# Optimizing a Trainium2 kernel written in Bass

```python
import numpy as np
import jax
import jax.numpy as jnp

def _softmax(x, axis=-1):
    return jax.nn.softmax(x, axis=axis)

def _gelu(x):
    return jax.nn.gelu(x, approximate=True)

def _silu(x):
    return jax.nn.silu(x)

def _sigmoid(x):
    return jax.nn.sigmoid(x)

def _layernorm(x, axis=-1, eps=1e-05):
    m = jnp.mean(x, axis=axis, keepdims=True)
    v = jnp.var(x, axis=axis, keepdims=True)
    return (x - m) / jnp.sqrt(v + eps)

def _scatter_add(tgt, idx, src, axis=0):
    return tgt.at[idx].add(src)

def _segment_sum(src, seg, n):
    return jax.ops.segment_sum(src, seg, n)
kernel_name = 'mk_rec_standalone_d1_rec_r8_2f0dd0'

def setup_inputs(seed: int=0):
    np.random.seed(seed)
    _w = jnp.asarray

    def _rec_inputs():
        import jax
        import jax.numpy as jnp
        _rk = jax.random.key(seed)
        r_x = -0.00011082 + 0.999858 * jax.random.normal(jax.random.fold_in(_rk, 1), (2048, 40, 128), jnp.float32)
        return r_x
    r_x = _rec_inputs()

    def _L0_rec_setup():
        import jax, jax.numpy as jnp
        import numpy as np
        key = jax.random.key(seed)
        k1, k2 = jax.random.split(key)
        B, F, D = (1024, 40, 128)
        x = jax.random.normal(k1, (B, F, D), dtype=jnp.float32)
        W = jax.random.normal(k2, (F, F), dtype=jnp.float32)
        return {'x': x, 'W': W}
    _L0_rec_all = _L0_rec_setup()
    _L0_rec_in = {k: v for k, v in _L0_rec_all.items() if k in ('W',)}
    del _L0_rec_all
    return {'r_x': r_x, 'L0_rec_W': _L0_rec_in['W']}

def reference(r_x, L0_rec_W):
    import jax
    import jax.numpy as jnp

    def _L0_rec_ref(x, W):
        import jax, jax.numpy as jnp
        import numpy as np
        F = x.shape[1]
        mask = jnp.triu(jnp.ones((F, F), dtype=x.dtype), k=1)
        gram = jnp.einsum('bfd,bgd->bfg', x, x)
        logit = jnp.einsum('bfg,fg->b', gram, W * mask)
        return logit[:, None]
    y = _L0_rec_ref(r_x, L0_rec_W)
    return y

_drawn_inputs = setup_inputs


def setup_inputs(seed=0):
    import zlib

    import numpy as np

    out = dict(_drawn_inputs(seed))
    spreads = {}
    factors = {}
    for name, (base, spread) in spreads.items():
        noise = np.random.default_rng([zlib.crc32(name.encode()), seed]).standard_normal(out[name].shape)
        drawn = base * np.exp(spread * noise) if base else spread * noise
        out[name] = jnp.asarray(drawn.astype(out[name].dtype))
    for name, factor in factors.items():
        out[name] = (out[name] * factor).astype(out[name].dtype)
    return out
```

```python
import concourse.bass as bass
from concourse import mybir
from contextlib import ExitStack


def masked_gram_logit_kernel(nc: bass.Bass, x: bass.AP, w: bass.AP, out: bass.AP):
    fp32 = mybir.dt.float32
    ALU = mybir.AluOpType
    ACT = mybir.ActivationFunctionType
    AX = mybir.AxisListType

    B, F, D = x.shape
    K = 128 // F
    LANES = K * F
    TRIPLES = B // K
    REST = B - K * TRIPLES
    BANK = 512
    G = 4 * BANK // D
    RING = 6
    PRODS = 3
    GROUPS = TRIPLES // G
    ROUNDS = GROUPS // RING
    TAIL = TRIPLES - GROUPS * G
    TAILW = TAIL + (1 if REST else 0)
    ON_ACT = 10
    TAIL_ON_ACT = 6
    SUMS = TRIPLES + (1 if REST else 0)
    PER = 6
    ROWS = -(-SUMS // PER)
    assert GROUPS == ROUNDS * RING and REST and ROUNDS > 1

    x_triples = x[0:K * TRIPLES, :, :].rearrange("(t k) f d -> (k f) t d", k=K)
    x_rest = x[K * TRIPLES:B, :, :].rearrange("b f d -> (b f) d")

    ctx = ExitStack()
    with ctx:
        def sb(name, shape):
            return ctx.enter_context(nc.sbuf_tensor(name, shape, fp32))

        def sem(name):
            return ctx.enter_context(nc.semaphore(name))

        weights = sb("weights", [LANES, LANES])
        x_ring = sb("x_ring", [LANES, RING, G, D])
        x_tail = sb("x_tail", [LANES, TAILW, D])
        products = sb("products", [LANES, PRODS, G, D])
        lane_sums = sb("lane_sums", [LANES, ROWS * PER])
        batch_ones = sb("batch_ones", [LANES, K])
        logits = sb("logits", [ROWS, PER * K])
        y = ctx.enter_context(nc.psum_tensor("y", [LANES, 2, G, D], fp32))
        totals = y[0:ROWS, 0, 0, 0:PER * K]

        weights_cleared = sem("weights_cleared")
        w_loaded = sem("w_loaded")
        weights_ready = sem("weights_ready")
        ones_filled = sem("ones_filled")
        ones_ready = sem("ones_ready")
        sums_padded = sem("sums_padded")
        x_loaded = [sem(f"x_loaded_{s}") for s in range(RING)]
        tail_cleared = sem("tail_cleared")
        tail_loaded = sem("tail_loaded")
        y_ready = sem("y_ready")
        multiplied = sem("multiplied")
        act_summed = sem("act_summed")
        dve_summed = sem("dve_summed")
        totals_ready = sem("totals_ready")
        logits_ready = sem("logits_ready")
        stored = sem("stored")

        block = ctx.enter_context(nc.Block())

        @block.sync
        def _(sp):
            def load(slot, first_triple):
                sp.dma_start(x_ring[:, slot, :, :], x_triples[:, bass.ds(first_triple, G), :])\
                  .then_inc(x_loaded[slot], 16)

            for s in range(RING):
                load(s, s * G)
            with sp.Fori(1, ROUNDS) as r:
                for s in range(RING):
                    sp.wait_ge(multiplied, (r - 1) * RING + s + 1)
                    load(s, (r * RING + s) * G)
            sp.dma_start(x_tail[:, 0:TAIL, :], x_triples[:, GROUPS * G:TRIPLES, :]).then_inc(tail_loaded, 16)
            sp.wait_ge(tail_cleared, 1)
            sp.dma_start(x_tail[0:REST * F, TAIL, :], x_rest).then_inc(tail_loaded, 16)
            sp.wait_ge(logits_ready, 1)
            full = B // (PER * K) // 16 * 16
            sp.dma_start(out[0:full * PER * K, :].rearrange("(p n) o -> p (n o)", n=PER * K),
                         logits[0:full, :]).then_inc(stored, 16)
            left = B - full * PER * K
            whole = left // (PER * K)
            sp.dma_start(out[full * PER * K:(full + whole) * PER * K, :].rearrange("(p n) o -> p (n o)", n=PER * K),
                         logits[full:full + whole, :]).then_inc(stored, 16)
            sp.dma_start(out[(full + whole) * PER * K:B, :].rearrange("(p n) o -> p (n o)", p=1),
                         logits[full + whole:full + whole + 1, 0:left - whole * PER * K]).then_inc(stored, 16)
            sp.wait_ge(stored, 48)

        @block.gpsimd
        def _(pool):
            pool.memset(weights[:, :], 0.0).then_inc(weights_cleared, 1)
            pool.memset(batch_ones[:, :], 1.0).then_inc(ones_filled, 1)
            pool.memset(x_tail[:, TAIL, :], 0.0).then_inc(tail_cleared, 1)
            pool.memset(lane_sums[:, SUMS:], 0.0).then_inc(sums_padded, 1)
            pool.wait_ge(w_loaded, 16 * K)
            pool.affine_select(out=weights[:, :], in_=weights[:, :], compare_op=ALU.is_gt, fill=0.0,
                               base=0, pattern=[[1, LANES]], channel_multiplier=-1).then_inc(weights_ready, 1)
            pool.wait_ge(ones_filled, 1)
            pool.affine_select(out=batch_ones[:, :], in_=batch_ones[:, :], compare_op=ALU.is_ge, fill=0.0,
                               base=0, pattern=[[-F, K]], channel_multiplier=1).then_inc(ones_filled, 1)
            pool.wait_ge(ones_filled, 2)
            pool.affine_select(out=batch_ones[:, :], in_=batch_ones[:, :], compare_op=ALU.is_gt, fill=0.0,
                               base=F, pattern=[[F, K]], channel_multiplier=-1).then_inc(ones_ready, 1)

        @block.tensor
        def _(pe):
            def columns(half, moving, triples):
                per = BANK // D
                for a in range(0, triples, per):
                    b = min(a + per, triples)
                    last = nc.tensor.matmul(y[:, half, a:b, :], weights[:, :], moving[:, a:b, :],
                                            start=True, stop=True)
                last.then_inc(y_ready, 1)

            pe.wait_ge(weights_ready, 1)
            for s in range(RING):
                pe.wait_ge(x_loaded[s], 16)
                if s >= 2:
                    pe.wait_ge(multiplied, s - 1)
                columns(s % 2, x_ring[:, s, :, :], G)
            with pe.Fori(1, ROUNDS) as r:
                for s in range(RING):
                    pe.wait_ge(x_loaded[s], (r + 1) * 16)
                    pe.wait_ge(multiplied, r * RING + s - 1)
                    columns(s % 2, x_ring[:, s, :, :], G)
            pe.wait_ge(tail_loaded, 32)
            pe.wait_ge(multiplied, GROUPS - 1)
            columns(GROUPS % 2, x_tail[:, :, :], TAILW)
            pe.wait_ge(ones_ready, 1)
            pe.wait_ge(sums_padded, 1)
            pe.wait_ge(act_summed, GROUPS + 1)
            pe.wait_ge(dve_summed, GROUPS + 1)
            by_row = lane_sums[:, :].rearrange("l (p i) -> l i p", i=PER)
            for i in range(PER):
                last = nc.tensor.matmul(totals[:, i * K:(i + 1) * K], by_row[:, i, :], batch_ones[:, :],
                                        start=True, stop=True)
            last.then_inc(totals_ready, 1)

        @block.vector
        def _(dve):
            def multiply(half, slot, moving, triples):
                nc.vector.tensor_tensor(products[:, slot, 0:triples, :], y[:, half, 0:triples, :], moving,
                                        ALU.mult).then_inc(multiplied, 1)

            def sum_share(slot, first, triples, first_sum):
                nc.vector.tensor_reduce(lane_sums[:, bass.ds(first_sum + first, triples - first)],
                                        products[:, slot, first:triples, :], AX.X, ALU.add)\
                  .then_inc(dve_summed, 1)

            for s in range(RING):
                dve.wait_ge(y_ready, s + 1)
                if s >= PRODS:
                    dve.wait_ge(act_summed, s - PRODS + 1)
                    dve.wait_ge(dve_summed, s - PRODS + 1)
                multiply(s % 2, s % PRODS, x_ring[:, s, :, :], G)
                if s >= 1:
                    dve.wait_ge(multiplied, s)
                    sum_share((s - 1) % PRODS, ON_ACT, G, (s - 1) * G)
            with dve.Fori(1, ROUNDS) as r:
                for s in range(RING):
                    dve.wait_ge(y_ready, r * RING + s + 1)
                    dve.wait_ge(act_summed, r * RING + s - PRODS + 1)
                    dve.wait_ge(dve_summed, r * RING + s - PRODS + 1)
                    multiply(s % 2, s % PRODS, x_ring[:, s, :, :], G)
                    dve.wait_ge(multiplied, r * RING + s)
                    sum_share((s - 1) % PRODS, ON_ACT, G, (r * RING + s - 1) * G)
            dve.wait_ge(y_ready, GROUPS + 1)
            dve.wait_ge(act_summed, GROUPS - PRODS + 1)
            dve.wait_ge(dve_summed, GROUPS - PRODS + 1)
            multiply(GROUPS % 2, GROUPS % PRODS, x_tail[:, :, :], TAILW)
            dve.wait_ge(multiplied, GROUPS)
            sum_share((GROUPS - 1) % PRODS, ON_ACT, G, (GROUPS - 1) * G)
            dve.wait_ge(multiplied, GROUPS + 1)
            sum_share(GROUPS % PRODS, TAIL_ON_ACT, TAILW, GROUPS * G)
            dve.wait_ge(totals_ready, 1)
            nc.vector.tensor_copy(logits[:, :], totals).then_inc(logits_ready, 1)

        @block.scalar
        def _(act):
            act.wait_ge(weights_cleared, 1)
            for k in range(K):
                act.dma_start(weights[k * F:(k + 1) * F, k * F:(k + 1) * F], w).then_inc(w_loaded, 16)

            def sum_share(slot, triples, first_sum):
                for j in range(triples):
                    last = nc.scalar.activation(products[:, slot, j, :], products[:, slot, j, :], ACT.Copy,
                                                accum_out=lane_sums[:, bass.ds(first_sum + j, 1)])
                last.then_inc(act_summed, 1)

            for s in range(RING):
                act.wait_ge(multiplied, s + 1)
                sum_share(s % PRODS, ON_ACT, s * G)
            with act.Fori(1, ROUNDS) as r:
                for s in range(RING):
                    act.wait_ge(multiplied, r * RING + s + 1)
                    sum_share(s % PRODS, ON_ACT, (r * RING + s) * G)
            act.wait_ge(multiplied, GROUPS + 1)
            sum_share(GROUPS % PRODS, TAIL_ON_ACT, GROUPS * G)


def kernel(**inputs):
    import numpy as _np
    import concourse.bacc as _bacc
    from concourse import mybir as _mybir
    from concourse.bass_utils import run_bass_kernel_spmd as _run

    nc = _bacc.Bacc("TRN2", target_bir_lowering=False, num_devices=1)
    arrays, args = {}, []
    for name in ("r_x", "L0_rec_W"):
        a = _np.ascontiguousarray(inputs[name])
        arrays[f"in_{name}_dram"] = a
        args.append(nc.dram_tensor(f"in_{name}_dram", a.shape, _mybir.dt.from_np(a.dtype), kind="ExternalInput").ap())
    args.append(nc.dram_tensor("out_0_dram", (inputs["r_x"].shape[0], 1), _mybir.dt.float32,
                               kind="ExternalOutput").ap())
    masked_gram_logit_kernel(nc, *args)
    r = _run(nc, [arrays], core_ids=[0])
    return r.results[0]["out_0_dram"]
```

```python
import concourse.bass as bass
from concourse import mybir
from contextlib import ExitStack


def masked_gram_logit_kernel(nc: bass.Bass, x: bass.AP, w: bass.AP, out: bass.AP):
    fp32 = mybir.dt.float32
    ALU = mybir.AluOpType
    ACT = mybir.ActivationFunctionType
    AX = mybir.AxisListType

    B, F, D = x.shape
    K = 128 // F
    LANES = K * F
    TRIPLES = B // K
    REST = B - K * TRIPLES
    BANK = 512
    STEPS = 2
    G = 4 * BANK // D
    STEP = G // STEPS
    PIECE = BANK // D
    RING = 6
    PRODS = 3
    FIRST = RING - 2
    ROUNDS = (TRIPLES // G - FIRST) // RING
    GROUPS = FIRST + ROUNDS * RING
    END = TRIPLES - GROUPS * G
    ENDW = END + 1
    HEADS = [(a, a + PIECE) for a in range(0, G, PIECE)]
    ENDS = [(a, min(a + PIECE, ENDW)) for a in range(0, ENDW, PIECE)]
    ON_ACT = 9
    END_ON_ACT = [2] * (len(ENDS) - 1) + [1]
    SHARED = [i for i, (a, b) in enumerate(ENDS) if END_ON_ACT[i] < b - a]
    BANKS = 2 * G // PIECE
    WARM = 10
    SUMS = TRIPLES + 1
    BULK = GROUPS * G
    ROWS = 128
    PER = BULK // ROWS
    assert REST and ROUNDS > 1 and SHARED[-1] == len(ENDS) - 1 and FIRST % 2 == 0 and BULK == ROWS * PER

    x_triples = x[0:K * TRIPLES, :, :].rearrange("(t k) f d -> (k f) t d", k=K)
    x_rest = x[K * TRIPLES:B, :, :].rearrange("b f d -> (b f) d")

    ctx = ExitStack()
    with ctx:
        def sb(name, shape):
            return ctx.enter_context(nc.sbuf_tensor(name, shape, fp32))

        def sem(name):
            return ctx.enter_context(nc.semaphore(name))

        w_blocks = sb("w_blocks", [LANES, LANES])
        mask = sb("mask", [LANES, LANES])
        weights = sb("weights", [LANES, LANES])
        x_ring = sb("x_ring", [LANES, RING, G, D])
        x_end = sb("x_end", [LANES, ENDW, D])
        products = sb("products", [LANES, PRODS, G, D])
        end_products = sb("end_products", [LANES, ENDW, D])
        lane_sums = sb("lane_sums", [LANES, SUMS])
        zeros = sb("zeros", [LANES, D])
        batch_ones = sb("batch_ones", [LANES, K])
        logits = sb("logits", [ROWS, PER * K])
        end_logits = sb("end_logits", [SUMS - BULK, K])
        psum = ctx.enter_context(nc.psum_tensor("psum", [128, 2, G, D], fp32))
        y = psum[0:LANES, :, :, :]
        by_bank = psum[:, :, :, :].rearrange("l h (c t) d -> l (h c) t d", t=PIECE)
        y_end = [by_bank[0:LANES, i % BANKS, 0:b - a, :] for i, (a, b) in enumerate(ENDS)]
        totals = by_bank[0:ROWS, len(ENDS) % BANKS, 0, 0:PER * K]
        end_totals = by_bank[0:SUMS - BULK, (len(ENDS) + 1) % BANKS, 0, 0:K]

        zeros_ready = sem("zeros_ready")
        w_loaded = sem("w_loaded")
        weights_ready = sem("weights_ready")
        mask_filled = sem("mask_filled")
        mask_ready = sem("mask_ready")
        ones_filled = sem("ones_filled")
        ones_ready = sem("ones_ready")
        head_loaded = [sem(f"head_loaded_{i}") for i in range(len(HEADS))]
        x_loaded = [sem(f"x_loaded_{s}") for s in range(RING)]
        end_cleared = sem("end_cleared")
        end_loaded = sem("end_loaded")
        y_ready = sem("y_ready")
        multiplied = sem("multiplied")
        act_summed = sem("act_summed")
        halved = sem("halved")
        dve_summed = sem("dve_summed")
        end_y_ready = sem("end_y_ready")
        end_multiplied = sem("end_multiplied")
        end_act_summed = sem("end_act_summed")
        end_halved = sem("end_halved")
        end_dve_summed = sem("end_dve_summed")
        totals_ready = sem("totals_ready")
        logits_ready = sem("logits_ready")
        stored = sem("stored")

        block = ctx.enter_context(nc.Block())

        @block.sync
        def _(sp):
            def load(slot, first_triple):
                sp.dma_start(x_ring[:, slot, :, :], x_triples[:, bass.ds(first_triple, G), :])\
                  .then_inc(x_loaded[slot], 16)

            for k in range(K):
                sp.dma_start(w_blocks[k * F:(k + 1) * F, :].rearrange("g (c f) -> g c f", c=K),
                             w.rearrange("g (c f) -> g c f", c=1).broadcast_to([F, K, F])).then_inc(w_loaded, 16)
            for i, (a, b) in enumerate(HEADS):
                sp.dma_start(x_ring[:, 0, a:b, :], x_triples[:, a:b, :]).then_inc(head_loaded[i], 16)
            for s in range(1, RING):
                load(s, s * G)
            with sp.Fori(0, ROUNDS - 1) as r:
                for s in range(RING):
                    sp.wait_ge(multiplied, (r * RING + s + 1) * STEPS)
                    load(s, (r * RING + RING + s) * G)
            for s in range(FIRST):
                sp.wait_ge(multiplied, ((ROUNDS - 1) * RING + s + 1) * STEPS)
                load(s, (ROUNDS * RING + s) * G)
            sp.dma_start(x_end[:, 0:END, :], x_triples[:, GROUPS * G:TRIPLES, :]).then_inc(end_loaded, 16)
            sp.wait_ge(end_cleared, 1)
            sp.dma_start(x_end[0:REST * F, END, :], x_rest).then_inc(end_loaded, 16)
            sp.wait_ge(logits_ready, 1)
            sp.dma_start(out[0:BULK * K, :].rearrange("(p n) o -> p (n o)", n=PER * K), logits[:, :])\
              .then_inc(stored, 16)
            sp.wait_ge(logits_ready, 2)
            sp.dma_start(out[BULK * K:TRIPLES * K, :].rearrange("(p n) o -> p (n o)", n=K),
                         end_logits[0:TRIPLES - BULK, :]).then_inc(stored, 16)
            sp.wait_ge(stored, 48)

        @block.gpsimd
        def _(pool):
            pool.memset(mask[:, :], 1.0).then_inc(mask_filled, 1)
            pool.memset(batch_ones[:, :], 1.0).then_inc(ones_filled, 1)
            pool.wait_ge(mask_filled, 1)
            pool.affine_select(out=mask[:, :], in_=mask[:, :], compare_op=ALU.is_gt, fill=0.0,
                               base=0, pattern=[[1, LANES]], channel_multiplier=-1).then_inc(mask_filled, 1)
            pool.wait_ge(mask_filled, 2)
            pool.affine_select(out=mask[:, :], in_=mask[:, :], compare_op=ALU.is_ge, fill=0.0,
                               base=0, pattern=[[-F, K], [0, F]], channel_multiplier=1).then_inc(mask_ready, 1)
            pool.memset(x_end[:, END, :], 0.0).then_inc(end_cleared, 1)
            pool.wait_ge(ones_filled, 1)
            pool.affine_select(out=batch_ones[:, :], in_=batch_ones[:, :], compare_op=ALU.is_ge, fill=0.0,
                               base=0, pattern=[[-F, K]], channel_multiplier=1).then_inc(ones_filled, 1)
            pool.wait_ge(ones_filled, 2)
            pool.affine_select(out=batch_ones[:, :], in_=batch_ones[:, :], compare_op=ALU.is_gt, fill=0.0,
                               base=F, pattern=[[F, K]], channel_multiplier=-1).then_inc(ones_ready, 1)

            def halve(prods):
                return nc.gpsimd.tensor_tensor(prods[:, :, 0:D // 2], prods[:, :, 0:D // 2], prods[:, :, D // 2:D],
                                               ALU.add)

            for g in range(FIRST):
                pool.wait_ge(multiplied, (g + 1) * STEPS)
                halve(products[:, g % PRODS, ON_ACT:G, :]).then_inc(halved, 1)
            with pool.Fori(0, ROUNDS) as r:
                for i in range(RING):
                    g = FIRST + i
                    pool.wait_ge(multiplied, (r * RING + g + 1) * STEPS)
                    halve(products[:, g % PRODS, ON_ACT:G, :]).then_inc(halved, 1)
            for i in SHARED[:-1]:
                a, b = ENDS[i][0] + END_ON_ACT[i], ENDS[i][1]
                pool.wait_ge(end_multiplied, i + 1)
                halve(end_products[:, a:b, :]).then_inc(end_halved, 1)

        @block.tensor
        def _(pe):
            def columns(into, moving):
                return nc.tensor.matmul(into, weights[:, :], moving, start=True, stop=True)

            def group(half, slot, multiplied_before):
                for a, b in HEADS:
                    if a % STEP == 0 and multiplied_before is not None:
                        pe.wait_ge(multiplied, multiplied_before + a // STEP + 1)
                    last = columns(y[:, half, a:b, :], x_ring[:, slot, a:b, :])
                    if b % STEP == 0:
                        last.then_inc(y_ready, 1)

            pe.wait_ge(zeros_ready, 1)
            for _ in range(WARM):
                nc.tensor.matmul(y[:, 1, 0, :], zeros[:, 0:LANES], zeros[:, :], start=True, stop=True)
            pe.wait_ge(weights_ready, 1)
            for i, (a, b) in enumerate(HEADS):
                pe.wait_ge(head_loaded[i], 16)
                last = columns(y[:, 0, a:b, :], x_ring[:, 0, a:b, :])
                if b % STEP == 0:
                    last.then_inc(y_ready, 1)
            for g in range(1, FIRST):
                pe.wait_ge(x_loaded[g], 16)
                group(g % 2, g, (g - 2) * STEPS if g >= 2 else None)
            with pe.Fori(0, ROUNDS) as r:
                for i in range(RING):
                    slot = (FIRST + i) % RING
                    pe.wait_ge(x_loaded[slot], r * 16 + (32 if 0 < slot < FIRST else 16))
                    group((FIRST + i) % 2, slot, (r * RING + FIRST + i - 2) * STEPS)
            pe.wait_ge(end_loaded, 32)
            for i, (a, b) in enumerate(ENDS):
                if i < BANKS and a % STEP == 0:
                    pe.wait_ge(multiplied, (GROUPS - 2) * STEPS + a // STEP + 1)
                elif i >= BANKS:
                    pe.wait_ge(end_multiplied, i - BANKS + 1)
                columns(y_end[i], x_end[:, a:b, :]).then_inc(end_y_ready, 1)
            pe.wait_ge(ones_ready, 1)
            pe.wait_ge(act_summed, GROUPS)
            pe.wait_ge(dve_summed, GROUPS)
            pe.wait_ge(end_multiplied, len(ENDS) - BANKS + 2)
            by_row = lane_sums[:, 0:BULK].rearrange("l (p i) -> l i p", i=PER)
            for i in range(PER):
                last = nc.tensor.matmul(totals[:, i * K:(i + 1) * K], by_row[:, i, :], batch_ones[:, :],
                                        start=True, stop=True)
            last.then_inc(totals_ready, 1)
            pe.wait_ge(end_act_summed, len(ENDS))
            pe.wait_ge(end_dve_summed, len(SHARED))
            nc.tensor.matmul(end_totals, lane_sums[:, BULK:SUMS], batch_ones[:, :],
                             start=True, stop=True).then_inc(totals_ready, 1)

        @block.vector
        def _(dve):
            def multiply(half, slot, prod, ready_before):
                for k in range(STEPS):
                    a, b = k * STEP, (k + 1) * STEP
                    dve.wait_ge(y_ready, ready_before + k + 1)
                    nc.vector.tensor_tensor(products[:, prod, a:b, :], y[:, half, a:b, :], x_ring[:, slot, a:b, :],
                                            ALU.mult).then_inc(multiplied, 1)

            def sum_halves(prod, first_sum):
                nc.vector.tensor_reduce(lane_sums[:, bass.ds(first_sum + ON_ACT, G - ON_ACT)],
                                        products[:, prod, ON_ACT:G, 0:D // 2], AX.X, ALU.add)\
                  .then_inc(dve_summed, 1)

            def end_share(i):
                if i == SHARED[-1]:
                    dve.wait_ge(end_multiplied, len(ENDS))
                else:
                    dve.wait_ge(end_halved, SHARED.index(i) + 1)
                width = D if i == SHARED[-1] else D // 2
                a, b = ENDS[i][0] + END_ON_ACT[i], ENDS[i][1]
                nc.vector.tensor_reduce(lane_sums[:, GROUPS * G + a:GROUPS * G + b], end_products[:, a:b, 0:width],
                                        AX.X, ALU.add).then_inc(end_dve_summed, 1)

            nc.vector.memset(zeros[:, :], 0.0).then_inc(zeros_ready, 1)
            dve.wait_ge(mask_ready, 1)
            dve.wait_ge(w_loaded, 16 * K)
            nc.vector.tensor_tensor(weights[:, :], w_blocks[:, :], mask[:, :], ALU.mult).then_inc(weights_ready, 1)
            for g in range(FIRST):
                if g >= PRODS:
                    dve.wait_ge(act_summed, g - PRODS + 1)
                    dve.wait_ge(dve_summed, g - PRODS + 1)
                multiply(g % 2, g, g % PRODS, g * STEPS)
                if g >= 1:
                    dve.wait_ge(halved, g)
                    sum_halves((g - 1) % PRODS, (g - 1) * G)
            with dve.Fori(0, ROUNDS) as r:
                for i in range(RING):
                    g = FIRST + i
                    dve.wait_ge(act_summed, r * RING + g - PRODS + 1)
                    dve.wait_ge(dve_summed, r * RING + g - PRODS + 1)
                    multiply(g % 2, g % RING, g % PRODS, (r * RING + g) * STEPS)
                    dve.wait_ge(halved, r * RING + g)
                    sum_halves((g - 1) % PRODS, (r * RING + g - 1) * G)
            for i, (a, b) in enumerate(ENDS):
                dve.wait_ge(end_y_ready, i + 1)
                nc.vector.tensor_tensor(end_products[:, a:b, :], y_end[i], x_end[:, a:b, :],
                                        ALU.mult).then_inc(end_multiplied, 1)
                if i == 0:
                    dve.wait_ge(halved, GROUPS)
                    sum_halves((GROUPS - 1) % PRODS, (GROUPS - 1) * G)
                elif i - 1 in SHARED:
                    end_share(i - 1)
            end_share(len(ENDS) - 1)
            dve.wait_ge(totals_ready, 1)
            nc.vector.tensor_copy(logits[:, :], totals).then_inc(logits_ready, 1)
            dve.wait_ge(totals_ready, 2)
            nc.vector.tensor_copy(end_logits[:, :], end_totals).then_inc(logits_ready, 1)

        @block.scalar
        def _(act):
            def sums(prods, triples, first_sum):
                for j in range(triples):
                    last = nc.scalar.activation(prods[:, j, :], prods[:, j, :], ACT.Copy,
                                                accum_out=lane_sums[:, bass.ds(first_sum + j, 1)])
                return last

            def group_sums(prod, group):
                for k in range(-(-ON_ACT // STEP)):
                    a, b = k * STEP, min((k + 1) * STEP, ON_ACT)
                    act.wait_ge(multiplied, group * STEPS + k + 1)
                    last = sums(products[:, prod, a:b, :], b - a, group * G + a)
                last.then_inc(act_summed, 1)

            for g in range(FIRST):
                group_sums(g % PRODS, g)
            with act.Fori(0, ROUNDS) as r:
                for i in range(RING):
                    g = FIRST + i
                    group_sums(g % PRODS, r * RING + g)
            for i, (a, b) in enumerate(ENDS):
                act.wait_ge(end_multiplied, i + 1)
                sums(end_products[:, a:b, :], END_ON_ACT[i], GROUPS * G + a).then_inc(end_act_summed, 1)
            act.wait_ge(logits_ready, 2)
            act.dma_start(out[TRIPLES * K:B, :].rearrange("(p n) o -> p (n o)", p=1),
                          end_logits[TRIPLES - BULK:SUMS - BULK, 0:REST]).then_inc(stored, 16)


def kernel(**inputs):
    import numpy as _np
    import concourse.bacc as _bacc
    from concourse import mybir as _mybir
    from concourse.bass_utils import run_bass_kernel_spmd as _run

    nc = _bacc.Bacc("TRN2", target_bir_lowering=False, num_devices=1)
    arrays, args = {}, []
    for name in ("r_x", "L0_rec_W"):
        a = _np.ascontiguousarray(inputs[name])
        arrays[f"in_{name}_dram"] = a
        args.append(nc.dram_tensor(f"in_{name}_dram", a.shape, _mybir.dt.from_np(a.dtype), kind="ExternalInput").ap())
    args.append(nc.dram_tensor("out_0_dram", (inputs["r_x"].shape[0], 1), _mybir.dt.float32,
                               kind="ExternalOutput").ap())
    masked_gram_logit_kernel(nc, *args)
    r = _run(nc, [arrays], core_ids=[0])
    return r.results[0]["out_0_dram"]
```
